# Optimizing a Trainium2 kernel written in Bass

```python
import numpy as np
import jax
import jax.numpy as jnp

def _softmax(x, axis=-1):
    return jax.nn.softmax(x, axis=axis)

def _gelu(x):
    return jax.nn.gelu(x, approximate=True)

def _silu(x):
    return jax.nn.silu(x)

def _sigmoid(x):
    return jax.nn.sigmoid(x)

def _layernorm(x, axis=-1, eps=1e-05):
    m = jnp.mean(x, axis=axis, keepdims=True)
    v = jnp.var(x, axis=axis, keepdims=True)
    return (x - m) / jnp.sqrt(v + eps)

def _scatter_add(tgt, idx, src, axis=0):
    return tgt.at[idx].add(src)

def _segment_sum(src, seg, n):
    return jax.ops.segment_sum(src, seg, n)
kernel_name = 'mk_rec_standalone_d1_rec_r8_b642ab'

def setup_inputs(seed: int=0):
    np.random.seed(seed)
    _w = jnp.asarray

    def _rec_inputs():
        import jax
        import jax.numpy as jnp
        _rk = jax.random.key(seed)
        r_embeddings = 8.78143e-05 + 1.00007 * jax.random.normal(jax.random.fold_in(_rk, 1), (2048, 27, 128), jnp.float32)
        return r_embeddings
    r_embeddings = _rec_inputs()

    def _L0_rec_setup():
        import jax, jax.numpy as jnp
        import numpy as np
        NUM_FEATURES = 27
        FEATURE_DIM = 128
        BATCH = 2048
        _TRIU_I, _TRIU_J = np.triu_indices(NUM_FEATURES, k=1)
        key = jax.random.key(seed)
        embeddings = jax.random.normal(key, (BATCH, NUM_FEATURES, FEATURE_DIM), dtype=jnp.float32)
        return {'embeddings': embeddings}
    _L0_rec_all = _L0_rec_setup()
    _L0_rec_in = {k: v for k, v in _L0_rec_all.items() if k in ()}
    del _L0_rec_all
    return {'r_embeddings': r_embeddings}

def reference(r_embeddings):
    import jax
    import jax.numpy as jnp

    def _L0_rec_ref(embeddings):
        import jax, jax.numpy as jnp
        import numpy as np
        NUM_FEATURES = 27
        FEATURE_DIM = 128
        BATCH = 2048
        _TRIU_I, _TRIU_J = np.triu_indices(NUM_FEATURES, k=1)
        B = embeddings.shape[0]
        interactions = jnp.einsum('bfd,bgd->bfg', embeddings, embeddings)
        flat_interactions = interactions[:, _TRIU_I, _TRIU_J]
        flat_embeddings = embeddings.reshape(B, -1)
        return jnp.concatenate([flat_embeddings, flat_interactions], axis=1)
    y = _L0_rec_ref(r_embeddings)
    return y

_drawn_inputs = setup_inputs


def setup_inputs(seed=0):
    import zlib

    import numpy as np

    out = dict(_drawn_inputs(seed))
    spreads = {}
    factors = {}
    for name, (base, spread) in spreads.items():
        noise = np.random.default_rng([zlib.crc32(name.encode()), seed]).standard_normal(out[name].shape)
        drawn = base * np.exp(spread * noise) if base else spread * noise
        out[name] = jnp.asarray(drawn.astype(out[name].dtype))
    for name, factor in factors.items():
        out[name] = (out[name] * factor).astype(out[name].dtype)
    return out
```

```python
from contextlib import ExitStack

import concourse.bass as bass
from concourse import mybir

F32 = mybir.dt.float32
ALU = mybir.AluOpType

P = 128
QUAD = 32
GROUP = P // QUAD
TILES_PER_SUPER = 4
BANK = 512


def build(nc, x, out):
    batches, feats, dim = x.shape
    assert dim == P and feats <= QUAD and batches % (P * TILES_PER_SUPER) == 0
    flat = feats * dim
    n_pairs = feats * (feats - 1) // 2
    firsts = feats - 1
    used = P - QUAD + firsts
    supers = batches // (P * TILES_PER_SUPER)
    assert supers >= 2
    groups = P // GROUP
    units = 4
    gram_unit = groups // units
    assert gram_unit * P == 2 * BANK
    tr_cut = [(feats * u + units - 1) // units for u in range(units + 1)]
    turn_cut = [(firsts * u + units - 1) // units for u in range(units + 1)]
    pair_at = [f * firsts - f * (f - 1) // 2 for f in range(feats)]
    fills = TILES_PER_SUPER * units + units

    with ExitStack() as ctx:
        def sb(name, shape):
            return ctx.enter_context(nc.sbuf_tensor(name, shape, F32))

        def sem(name):
            return ctx.enter_context(nc.semaphore(name))

        ident = sb("ident", [P, P])
        tile_x = [sb(f"tile_x{s}", [P, feats, dim]) for s in range(TILES_PER_SUPER)]
        xT = [sb(f"xT{s}", [P, P, QUAD]) for s in range(2)]
        gram = sb("gram", [P, TILES_PER_SUPER * groups, firsts])
        pairs = sb("pairs", [P, GROUP, n_pairs])
        tr_ps = [ctx.enter_context(nc.psum_tensor(f"tr_ps{s}", [P, 2, BANK // P, P], F32)) for s in range(2)]
        gram_ps = [ctx.enter_context(nc.psum_tensor(f"gram_ps{s}", [P, gram_unit, P], F32)) for s in range(2)]

        ident_zero = sem("ident_zero")
        consts_ready = sem("consts_ready")
        first_chunk = [sem(f"first_chunk{u}") for u in range(units)]
        x_loaded = [sem(f"x_loaded{s}") for s in range(TILES_PER_SUPER)]
        x_stored = [sem(f"x_stored{s}") for s in range(TILES_PER_SUPER)]
        tr_filled = sem("tr_filled")
        tr_copied = [sem(f"tr_copied{s}") for s in range(2)]
        gram_filled = sem("gram_filled")
        gram_copied = [sem(f"gram_copied{s}") for s in range(2)]
        pairs_stored = sem("pairs_stored")
        last_pairs_stored = sem("last_pairs_stored")
        pairs_free = sem("pairs_free")

        def rows(ap, tile):
            return ap[bass.ds(tile * P, P)]

        def halves(u):
            f0, f1 = tr_cut[u], tr_cut[u + 1]
            mid = f0 + (f1 - f0) // 2
            return (f0, mid), (mid, f1)

        def tr_fill(i, pos):
            return pos % 2, fills // 2 * i + pos // 2

        def turn_pos(final):
            return TILES_PER_SUPER * units if final else fills + 1

        def wait_pairs(eng, i, final):
            for u in (units - 2, units - 1):
                slot, uses = tr_fill(i, turn_pos(final) + u)
                eng.wait_ge(tr_copied[slot], 2 * (uses + 1))

        def pair_rows(i):
            dst = out[bass.ds(i * (P * TILES_PER_SUPER), P * TILES_PER_SUPER)]
            return dst.rearrange("(t b) n -> t b n", b=GROUP)[:, :, flat:flat + n_pairs]

        block = ctx.enter_context(nc.Block())

        @block.sync
        def _(sp):
            def load(tile, slot):
                sp.dma_start(tile_x[slot][:], rows(x, tile)).then_inc(x_loaded[slot], 16)

            def store(tile, slot):
                dst = rows(out, tile)[:, 0:flat].rearrange("p (f d) -> p f d", f=feats)
                sp.dma_start(dst, tile_x[slot][:]).then_inc(x_stored[slot], 16)

            for u in range(units):
                f0, f1 = tr_cut[u], tr_cut[u + 1]
                sp.dma_start(tile_x[0][:, f0:f1, :], x[0:P, f0:f1, :]).then_inc(first_chunk[u], 16)
            for s in range(1, TILES_PER_SUPER):
                load(s, s)
            for u in range(units):
                sp.wait_ge(first_chunk[u], 16)
            store(0, 0)
            with sp.Fori(0, supers - 1) as i:
                for m in range(1, TILES_PER_SUPER + 1):
                    slot, before = m % TILES_PER_SUPER, m - 1
                    sp.wait_ge(x_loaded[slot], 16 * i + 16)
                    store(4 * i + m, slot)
                    sp.wait_ge(tr_filled, fills * i + 4 * before + 4)
                    sp.wait_ge(x_stored[before], 16 * i + 16)
                    load(4 * i + m + 3, before)
            for m in range(1, TILES_PER_SUPER):
                sp.wait_ge(x_loaded[m], 16 * supers)
                store(4 * (supers - 1) + m, m)
            wait_pairs(sp, supers - 1, True)
            sp.dma_start(pair_rows(supers - 1), pairs[:]).then_inc(last_pairs_stored, 16)
            sp.wait_ge(last_pairs_stored, 16)
            for s in range(TILES_PER_SUPER):
                sp.wait_ge(x_stored[s], 16 * supers)

        @block.gpsimd
        def _(pool):
            nc.gpsimd.memset(ident[:], 0.0).then_inc(ident_zero, 1)
            pool.wait_ge(ident_zero, 1)
            nc.gpsimd.affine_select(out=ident[:], in_=ident[:], compare_op=ALU.not_equal, fill=1.0, base=0,
                                    pattern=[[-1, P]], channel_multiplier=1).then_inc(consts_ready, 1)
            for s in range(2):
                nc.gpsimd.memset(xT[s][:, :, feats:QUAD], 0.0).then_inc(consts_ready, 1)

            pool.sem_inc(pairs_free, 1)
            with pool.Fori(0, supers - 1) as i:
                wait_pairs(pool, i, False)
                pool.dma_start(pair_rows(i), pairs[:]).then_inc(pairs_stored, 16)
                pool.wait_ge(pairs_stored, 16 * i + 16)
                pool.sem_inc(pairs_free, 1)

        @block.tensor
        def _(pe):
            def transpose_unit(i, m, u):
                slot, uses = tr_fill(i, 4 * m + u)
                s = m % TILES_PER_SUPER
                pe.wait_ge(tr_copied[slot], 2 * uses)
                for half, (f0, f1) in enumerate(halves(u)):
                    for f in range(f0, f1):
                        last = nc.tensor.transpose(tr_ps[slot][:, half, f - f0, :], tile_x[s][:, f, :], ident[:])
                last.then_inc(tr_filled, 1)

            def gram_products(i, m, u):
                slot = u % 2
                pe.wait_ge(gram_copied[slot], 2 * (2 * (4 * i + m) + u // 2))
                src = xT[m % 2]
                for q in range(gram_unit):
                    b0 = (u * gram_unit + q) * GROUP
                    four = src[:, b0:b0 + GROUP, :]
                    last = nc.tensor.matmul(gram_ps[slot][0:used, q, 0:GROUP * firsts],
                                            four.rearrange("p b f -> p (b f)")[:, 1:1 + used],
                                            four[:, :, 0:firsts],
                                            start=True, stop=True)
                last.then_inc(gram_filled, 1)

            def wait_xT(i, m):
                for u in (units - 2, units - 1):
                    slot, uses = tr_fill(i, 4 * m + u)
                    pe.wait_ge(tr_copied[slot], 2 * (uses + 1))

            def turn_unit(i, u, final):
                slot, uses = tr_fill(i, turn_pos(final) + u)
                pe.wait_ge(tr_copied[slot], 2 * uses)
                for f in range(turn_cut[u], turn_cut[u + 1]):
                    n = f - turn_cut[u]
                    last = nc.tensor.transpose(tr_ps[slot][:, n // 4, n % 4, 0:used], gram[0:used, :, f],
                                               ident[0:used, 0:used])
                last.then_inc(tr_filled, 1)

            def supertile(i, final):
                for m in range(TILES_PER_SUPER):
                    for u in range(units):
                        if (m, u) >= (0, 2):
                            if u == 0:
                                wait_xT(i, m)
                            gram_products(i, m, u)
                        if (m, u) < (0, 1):
                            continue
                        ahead, v = m + 1 + (u + 1) // units, (u + 1) % units
                        if final and ahead >= TILES_PER_SUPER:
                            continue
                        if v == 0:
                            s = ahead % TILES_PER_SUPER
                            arrived = 16 * (ahead // TILES_PER_SUPER) + (0 if s == 0 else 16)
                            pe.wait_ge(x_loaded[s], 16 * i + arrived)
                        transpose_unit(i, ahead, v)
                if not final:
                    wait_xT(i, TILES_PER_SUPER)
                    gram_products(i, TILES_PER_SUPER, 0)
                for slot in range(2):
                    pe.wait_ge(gram_copied[slot], 2 * (2 * TILES_PER_SUPER * (i + 1)))
                for u in range(units):
                    turn_unit(i, u, final)
                if not final:
                    transpose_unit(i + 1, 1, 1)
                    gram_products(i, TILES_PER_SUPER, 1)

            pe.wait_ge(consts_ready, 3)
            for u in range(units):
                pe.wait_ge(first_chunk[u], 16)
                transpose_unit(0, 0, u)
            wait_xT(0, 0)
            gram_products(0, 0, 0)
            gram_products(0, 0, 1)
            pe.wait_ge(x_loaded[1], 16)
            transpose_unit(0, 1, 0)
            transpose_unit(0, 1, 1)
            with pe.Fori(0, supers - 1) as i:
                supertile(i, False)
            supertile(supers - 1, True)

        def copy_program(eng, copy, me):
            quads = (2 * me, 2 * me + 1)

            def copy_transposes(i, m, u):
                slot, _ = tr_fill(i, 4 * m + u)
                if u == 0 and not (isinstance(i, int) and 4 * i + m < 2):
                    eng.wait_ge(gram_filled, 16 * i + 4 * m - 4)
                eng.wait_ge(tr_filled, fills * i + 4 * m + u + 1)
                f0, f1 = halves(u)[me]
                copy(xT[m % 2][:, :, f0:f1],
                     tr_ps[slot][:, me, 0:f1 - f0, :].rearrange("p f b -> p b f")).then_inc(tr_copied[slot], 1)

            def copy_blocks(i, m, u):
                slot = u % 2
                eng.wait_ge(gram_filled, 16 * i + 4 * m + u + 1)
                t0 = (m % TILES_PER_SUPER) * groups + u * gram_unit
                for b in quads:
                    part = slice(b * QUAD, min(b * QUAD + QUAD, used))
                    last = copy(gram[part, t0:t0 + gram_unit, :],
                                gram_ps[slot][part, :, b * firsts:(b + 1) * firsts])
                last.then_inc(gram_copied[slot], 1)

            def copy_turns(i, u, final):
                slot, _ = tr_fill(i, turn_pos(final) + u)
                if u == 0:
                    eng.wait_ge(pairs_free, i + 1)
                eng.wait_ge(tr_filled, fills * i + turn_pos(final) + u + 1)
                mine = [f for f in range(turn_cut[u], turn_cut[u + 1]) if (f - turn_cut[u]) // 4 == me]
                for f in mine:
                    n = f - turn_cut[u]
                    src = tr_ps[slot][:, n // 4, n % 4, :].rearrange("p (b g) -> p b g", b=GROUP)
                    last = copy(pairs[:, :, pair_at[f]:pair_at[f] + firsts - f], src[:, :, f:firsts])
                last.then_inc(tr_copied[slot], 1)

            return copy_transposes, copy_blocks, copy_turns

        def run_copies(eng, copy, me):
            copy_transposes, copy_blocks, copy_turns = copy_program(eng, copy, me)

            def supertile(i, final):
                for m in range(TILES_PER_SUPER):
                    for u in range(units):
                        if (m, u) >= (0, 2):
                            copy_blocks(i, m, u)
                        if (m, u) < (0, 1):
                            continue
                        ahead, v = m + 1 + (u + 1) // units, (u + 1) % units
                        if final and ahead >= TILES_PER_SUPER:
                            continue
                        copy_transposes(i, ahead, v)
                for u in range(units):
                    copy_turns(i, u, final)
                if not final:
                    copy_blocks(i, TILES_PER_SUPER, 0)
                    copy_transposes(i + 1, 1, 1)
                    copy_blocks(i, TILES_PER_SUPER, 1)

            for u in range(units):
                copy_transposes(0, 0, u)
            copy_blocks(0, 0, 0)
            copy_blocks(0, 0, 1)
            copy_transposes(0, 1, 0)
            copy_transposes(0, 1, 1)
            with eng.Fori(0, supers - 1) as i:
                supertile(i, False)
            supertile(supers - 1, True)

        @block.vector
        def _(dve):
            run_copies(dve, nc.vector.tensor_copy, 0)

        @block.scalar
        def _(act):
            run_copies(act, nc.scalar.copy, 1)


def kernel(r_embeddings):
    import numpy as np
    import concourse.bacc as bacc
    from concourse.bass_utils import run_bass_kernel_spmd

    x = np.ascontiguousarray(r_embeddings)
    batches, feats, dim = x.shape
    width = feats * dim + feats * (feats - 1) // 2
    nc = bacc.Bacc("TRN2", target_bir_lowering=False, num_devices=1)
    x_dram = nc.dram_tensor("in_x_dram", x.shape, mybir.dt.from_np(x.dtype), kind="ExternalInput").ap()
    out_dram = nc.dram_tensor("out_dram", (batches, width), F32, kind="ExternalOutput").ap()
    build(nc, x_dram, out_dram)
    result = run_bass_kernel_spmd(nc, [{"in_x_dram": x}], core_ids=[0])
    return result.results[0]["out_dram"]
```

```python
from contextlib import ExitStack

import concourse.bass as bass
from concourse import mybir

F32 = mybir.dt.float32
ALU = mybir.AluOpType

P = 128
GROUP = 4
TILES_PER_SUPER = 4
BANK = 512


def build(nc, x, out):
    batches, feats, dim = x.shape
    assert dim == P and GROUP * feats <= P and batches % (P * TILES_PER_SUPER) == 0
    flat = feats * dim
    n_pairs = feats * (feats - 1) // 2
    firsts = feats - 1
    cols = GROUP * firsts
    used = GROUP * feats - 1
    supers = batches // (P * TILES_PER_SUPER)
    assert supers >= 2
    groups = P // GROUP
    units = 4
    gram_unit = groups // units
    assert gram_unit * P == 2 * BANK
    tr_cut = [(feats * u + units - 1) // units for u in range(units + 1)]
    half_cut = [0, tr_cut[units // 2], feats]
    follow = [(0,), (1,), (2, 3), ()]
    turn_cut = [(firsts * u + units - 1) // units for u in range(units + 1)]
    pair_at = [f * firsts - f * (f - 1) // 2 for f in range(feats)]
    fills = TILES_PER_SUPER * units + units

    with ExitStack() as ctx:
        def sb(name, shape):
            return ctx.enter_context(nc.sbuf_tensor(name, shape, F32))

        def sem(name):
            return ctx.enter_context(nc.semaphore(name))

        ident = sb("ident", [P, P])
        tile_x = [sb(f"tile_x{s}", [P, feats, dim]) for s in range(TILES_PER_SUPER)]
        xT = [sb(f"xT{s}", [P, P, feats]) for s in range(2)]
        gram = sb("gram", [used, TILES_PER_SUPER * groups, firsts])
        pairs = sb("pairs", [P, GROUP, n_pairs])
        tr_ps = [ctx.enter_context(nc.psum_tensor(f"tr_ps{s}", [P, 2, BANK // P, P], F32)) for s in range(2)]
        gram_ps = [ctx.enter_context(nc.psum_tensor(f"gram_ps{s}", [P, gram_unit, P], F32)) for s in range(2)]

        ident_zero = sem("ident_zero")
        consts_ready = sem("consts_ready")
        first_chunk = [sem(f"first_chunk{u}") for u in range(units)]
        x_loaded = [[sem(f"x_loaded{s}_{h}") for h in range(2)] for s in range(TILES_PER_SUPER)]
        x_stored = [[sem(f"x_stored{s}_{h}") for h in range(2)] for s in range(TILES_PER_SUPER)]
        tr_filled = sem("tr_filled")
        tr_copied = [sem(f"tr_copied{s}") for s in range(2)]
        gram_filled = sem("gram_filled")
        gram_copied = [sem(f"gram_copied{s}") for s in range(2)]
        block_copied = [sem(f"block_copied{n}") for n in range(2)]
        pairs_stored = sem("pairs_stored")
        last_pairs_stored = sem("last_pairs_stored")
        pairs_free = sem("pairs_free")

        def rows(ap, tile):
            return ap[bass.ds(tile * P, P)]

        def halves(u):
            f0, f1 = tr_cut[u], tr_cut[u + 1]
            mid = f0 + (f1 - f0) // 2
            return (f0, mid), (mid, f1)

        def tr_fill(i, pos):
            return pos % 2, fills // 2 * i + pos // 2

        def turn_pos(final):
            return TILES_PER_SUPER * units if final else fills

        def wait_pairs(eng, i, final):
            for u in (units - 2, units - 1):
                slot, uses = tr_fill(i, turn_pos(final) + u)
                eng.wait_ge(tr_copied[slot], 2 * (uses + 1))

        def pair_rows(i):
            dst = out[bass.ds(i * (P * TILES_PER_SUPER), P * TILES_PER_SUPER)]
            return dst.rearrange("(t b) n -> t b n", b=GROUP)[:, :, flat:flat + n_pairs]

        block = ctx.enter_context(nc.Block())

        @block.sync
        def _(sp):
            def load(tile, slot, h):
                f0, f1 = half_cut[h], half_cut[h + 1]
                sp.dma_start(tile_x[slot][:, f0:f1, :], rows(x, tile)[:, f0:f1, :]).then_inc(x_loaded[slot][h], 16)

            def store(tile, slot, h):
                f0, f1 = half_cut[h], half_cut[h + 1]
                dst = rows(out, tile)[:, f0 * dim:f1 * dim].rearrange("p (f d) -> p f d", f=f1 - f0)
                sp.dma_start(dst, tile_x[slot][:, f0:f1, :]).then_inc(x_stored[slot][h], 16)

            for u in range(units):
                f0, f1 = tr_cut[u], tr_cut[u + 1]
                sp.dma_start(tile_x[0][:, f0:f1, :], x[0:P, f0:f1, :]).then_inc(first_chunk[u], 16)
            for s in range(1, TILES_PER_SUPER):
                for h in range(2):
                    load(s, s, h)
            for h in range(2):
                for u in range(2 * h, 2 * h + 2):
                    sp.wait_ge(first_chunk[u], 16)
                store(0, 0, h)
            with sp.Fori(0, supers - 1) as i:
                for m in range(1, TILES_PER_SUPER + 1):
                    slot, before = m % TILES_PER_SUPER, m - 1
                    for h in range(2):
                        sp.wait_ge(tr_filled, fills * i + 4 * before + 2 * h + 2)
                        sp.wait_ge(x_stored[before][h], 16 * i + 16)
                        load(4 * i + m + 3, before, h)
                        sp.wait_ge(x_loaded[slot][h], 16 * i + 16)
                        store(4 * i + m, slot, h)
            for m in range(1, TILES_PER_SUPER):
                for h in range(2):
                    sp.wait_ge(x_loaded[m][h], 16 * supers)
                    store(4 * (supers - 1) + m, m, h)
            wait_pairs(sp, supers - 1, True)
            sp.dma_start(pair_rows(supers - 1), pairs[:]).then_inc(last_pairs_stored, 16)
            sp.wait_ge(last_pairs_stored, 16)
            for s in range(TILES_PER_SUPER):
                for h in range(2):
                    sp.wait_ge(x_stored[s][h], 16 * supers)

        @block.gpsimd
        def _(pool):
            nc.gpsimd.memset(ident[:], 0.0).then_inc(ident_zero, 1)
            pool.wait_ge(ident_zero, 1)
            nc.gpsimd.affine_select(out=ident[:], in_=ident[:], compare_op=ALU.not_equal, fill=1.0, base=0,
                                    pattern=[[-1, P]], channel_multiplier=1).then_inc(consts_ready, 1)

            pool.sem_inc(pairs_free, 1)
            with pool.Fori(0, supers - 1) as i:
                wait_pairs(pool, i, False)
                pool.dma_start(pair_rows(i), pairs[:]).then_inc(pairs_stored, 16)
                pool.wait_ge(pairs_stored, 16 * i + 16)
                pool.sem_inc(pairs_free, 1)

        @block.tensor
        def _(pe):
            def transpose_unit(i, m, u):
                slot, uses = tr_fill(i, 4 * m + u)
                s = m % TILES_PER_SUPER
                if u % 2 == 0 and not (isinstance(i, int) and 4 * i + m == 0):
                    pe.wait_ge(x_loaded[s][u // 2], 16 * i + 16)
                pe.wait_ge(tr_copied[slot], 2 * uses)
                for half, (f0, f1) in enumerate(halves(u)):
                    for f in range(f0, f1):
                        last = nc.tensor.transpose(tr_ps[slot][:, half, f - f0, :], tile_x[s][:, f, :], ident[:])
                last.then_inc(tr_filled, 1)

            def gram_products(i, m, u):
                slot = u % 2
                pe.wait_ge(gram_copied[slot], 2 * (4 * i + m) + u // 2)
                src = xT[m % 2]
                for q in range(gram_unit):
                    b0 = (u * gram_unit + q) * GROUP
                    four = src[:, b0:b0 + GROUP, :]
                    rows_of_four = four.rearrange("p b f -> p (b f)")[:, 1:GROUP * feats]
                    last = nc.tensor.matmul(gram_ps[slot][0:used, q, 0:cols], rows_of_four,
                                            four[:, :, 0:firsts], start=True, stop=True)
                last.then_inc(gram_filled, 1)

            def wait_xT(i, m):
                for u in (units - 2, units - 1):
                    slot, uses = tr_fill(i, 4 * m + u)
                    pe.wait_ge(tr_copied[slot], 2 * (uses + 1))

            def turn_unit(i, u, final):
                slot, uses = tr_fill(i, turn_pos(final) + u)
                pe.wait_ge(tr_copied[slot], 2 * uses)
                for f in range(turn_cut[u], turn_cut[u + 1]):
                    n = f - turn_cut[u]
                    last = nc.tensor.transpose(tr_ps[slot][:, n // 4, n % 4, 0:used], gram[0:used, :, f],
                                               ident[0:used, 0:used])
                last.then_inc(tr_filled, 1)

            def gram_and_ahead(i, m, u, final):
                if u == 0:
                    wait_xT(i, m)
                gram_products(i, m, u)
                if not (final and m == TILES_PER_SUPER - 1):
                    for v in follow[u]:
                        transpose_unit(i, m + 1, v)

            def supertile(i, final):
                transpose_unit(i, 1, 1)
                for u in range(2, units):
                    gram_and_ahead(i, 0, u, final)
                for m in range(1, TILES_PER_SUPER):
                    for u in range(units):
                        gram_and_ahead(i, m, u, final)
                if not final:
                    wait_xT(i, TILES_PER_SUPER)
                    gram_products(i, TILES_PER_SUPER, 0)
                for slot in range(2):
                    pe.wait_ge(gram_copied[slot], 2 * TILES_PER_SUPER * (i + 1))
                for u in range(units):
                    turn_unit(i, u, final)
                if not final:
                    transpose_unit(i + 1, 1, 0)
                    gram_products(i, TILES_PER_SUPER, 1)

            pe.wait_ge(consts_ready, 1)
            for u in range(units):
                pe.wait_ge(first_chunk[u], 16)
                transpose_unit(0, 0, u)
            wait_xT(0, 0)
            gram_products(0, 0, 0)
            transpose_unit(0, 1, 0)
            gram_products(0, 0, 1)
            with pe.Fori(0, supers - 1) as i:
                supertile(i, False)
            supertile(supers - 1, True)

        def copy_program(eng, copy, me):
            block_rows = [(b, P // 2 if b * feats >= P // 2 else 0, b * feats + firsts)
                          for b in reversed(range(GROUP))]

            def copy_transposes(i, m, u):
                slot, _ = tr_fill(i, 4 * m + u)
                if u == 0 and not (isinstance(i, int) and 4 * i + m < 2):
                    eng.wait_ge(gram_filled, 16 * i + 4 * m - 4)
                eng.wait_ge(tr_filled, fills * i + 4 * m + u + 1)
                f0, f1 = halves(u)[me]
                copy(xT[m % 2][:, :, f0:f1],
                     tr_ps[slot][:, me, 0:f1 - f0, :].rearrange("p f b -> p b f")).then_inc(tr_copied[slot], 1)

            def copy_blocks(i, m, u):
                slot = u % 2
                if slot != me:
                    return
                eng.wait_ge(gram_filled, 16 * i + 4 * m + u + 1)
                t0 = (m % TILES_PER_SUPER) * groups + u * gram_unit
                before = (GROUP - 1) * (2 * (4 * i + m) + u // 2)
                for n, (b, p0, p1) in enumerate(block_rows):
                    if n:
                        eng.wait_ge(block_copied[me], before + n)
                    copy(gram[p0:p1, t0:t0 + gram_unit, :],
                         gram_ps[slot][p0:p1, :, b * firsts:(b + 1) * firsts]
                         ).then_inc(block_copied[me] if n < GROUP - 1 else gram_copied[slot], 1)

            def copy_turns(i, u, final):
                slot, _ = tr_fill(i, turn_pos(final) + u)
                if u == 0:
                    eng.wait_ge(pairs_free, i + 1)
                eng.wait_ge(tr_filled, fills * i + turn_pos(final) + u + 1)
                mine = [f for f in range(turn_cut[u], turn_cut[u + 1]) if (f - turn_cut[u]) // 4 == me]
                for f in mine:
                    n = f - turn_cut[u]
                    src = tr_ps[slot][:, n // 4, n % 4, 0:GROUP * feats].rearrange("p (b g) -> p b g", b=GROUP)
                    last = copy(pairs[:, :, pair_at[f]:pair_at[f] + firsts - f], src[:, :, f:firsts])
                last.then_inc(tr_copied[slot], 1)

            return copy_transposes, copy_blocks, copy_turns

        def run_copies(eng, copy, me):
            copy_transposes, copy_blocks, copy_turns = copy_program(eng, copy, me)

            def blocks_and_ahead(i, m, u, final):
                copy_blocks(i, m, u)
                if not (final and m == TILES_PER_SUPER - 1):
                    for v in follow[u]:
                        copy_transposes(i, m + 1, v)

            def supertile(i, final):
                copy_transposes(i, 1, 1)
                for u in range(2, units):
                    blocks_and_ahead(i, 0, u, final)
                for m in range(1, TILES_PER_SUPER):
                    for u in range(units):
                        blocks_and_ahead(i, m, u, final)
                for u in range(units):
                    copy_turns(i, u, final)
                if not final:
                    copy_blocks(i, TILES_PER_SUPER, 0)
                    copy_transposes(i + 1, 1, 0)
                    copy_blocks(i, TILES_PER_SUPER, 1)

            for u in range(units):
                copy_transposes(0, 0, u)
            copy_blocks(0, 0, 0)
            copy_transposes(0, 1, 0)
            copy_blocks(0, 0, 1)
            with eng.Fori(0, supers - 1) as i:
                supertile(i, False)
            supertile(supers - 1, True)

        @block.vector
        def _(dve):
            run_copies(dve, nc.vector.tensor_copy, 0)

        @block.scalar
        def _(act):
            run_copies(act, nc.scalar.copy, 1)


def kernel(r_embeddings):
    import numpy as np
    import concourse.bacc as bacc
    from concourse.bass_utils import run_bass_kernel_spmd

    x = np.ascontiguousarray(r_embeddings)
    batches, feats, dim = x.shape
    width = feats * dim + feats * (feats - 1) // 2
    nc = bacc.Bacc("TRN2", target_bir_lowering=False, num_devices=1)
    x_dram = nc.dram_tensor("in_x_dram", x.shape, mybir.dt.from_np(x.dtype), kind="ExternalInput").ap()
    out_dram = nc.dram_tensor("out_dram", (batches, width), F32, kind="ExternalOutput").ap()
    build(nc, x_dram, out_dram)
    result = run_bass_kernel_spmd(nc, [{"in_x_dram": x}], core_ids=[0])
    return result.results[0]["out_dram"]
```
